# Optimizing a Trainium2 kernel written in Bass

```python
import numpy as np
import jax
import jax.numpy as jnp

def _softmax(x, axis=-1):
    return jax.nn.softmax(x, axis=axis)

def _gelu(x):
    return jax.nn.gelu(x, approximate=True)

def _silu(x):
    return jax.nn.silu(x)

def _sigmoid(x):
    return jax.nn.sigmoid(x)

def _layernorm(x, axis=-1, eps=1e-05):
    m = jnp.mean(x, axis=axis, keepdims=True)
    v = jnp.var(x, axis=axis, keepdims=True)
    return (x - m) / jnp.sqrt(v + eps)

def _scatter_add(tgt, idx, src, axis=0):
    return tgt.at[idx].add(src)

def _segment_sum(src, seg, n):
    return jax.ops.segment_sum(src, seg, n)
kernel_name = 'mk_rec_standalone_d1_rec_r8_607844'

def setup_inputs(seed: int=0):
    np.random.seed(seed)
    _w = jnp.asarray

    def _rec_inputs():
        import jax
        import jax.numpy as jnp
        _rk = jax.random.key(seed)
        r_feature_emb = -0.000292821 + 1.00034 * jax.random.normal(jax.random.fold_in(_rk, 1), (2048, 32, 64), jnp.float32)
        return r_feature_emb
    r_feature_emb = _rec_inputs()

    def _L0_rec_setup():
        import jax, jax.numpy as jnp
        import numpy as np
        NUM_FIELDS = 32
        EMBED_DIM = 64
        INTERACT_DIM = NUM_FIELDS * (NUM_FIELDS - 1) // 2
        key = jax.random.key(seed)
        k1, k2 = jax.random.split(key)
        feature_emb = jax.random.normal(k1, (256, NUM_FIELDS, EMBED_DIM), dtype=jnp.float32)
        std = float(np.sqrt(2.0 / (EMBED_DIM + EMBED_DIM)))
        bilinear_W = jax.random.normal(k2, (INTERACT_DIM, EMBED_DIM, EMBED_DIM), dtype=jnp.float32) * std
        return {'feature_emb': feature_emb, 'bilinear_W': bilinear_W}
    _L0_rec_all = _L0_rec_setup()
    _L0_rec_in = {k: v for k, v in _L0_rec_all.items() if k in ('bilinear_W',)}
    del _L0_rec_all
    return {'r_feature_emb': r_feature_emb, 'L0_rec_bilinear_W': _L0_rec_in['bilinear_W']}

def reference(r_feature_emb, L0_rec_bilinear_W):
    import jax
    import jax.numpy as jnp

    def _L0_rec_ref(feature_emb, bilinear_W):
        import jax, jax.numpy as jnp
        import numpy as np
        NUM_FIELDS = 32
        EMBED_DIM = 64
        INTERACT_DIM = NUM_FIELDS * (NUM_FIELDS - 1) // 2
        nf = feature_emb.shape[1]
        i_idx, j_idx = jnp.triu_indices(nf, k=1)
        v_i = feature_emb[:, i_idx, :]
        v_j = feature_emb[:, j_idx, :]
        proj = jnp.einsum('bpd,pde->bpe', v_i, bilinear_W)
        return proj * v_j
    y = _L0_rec_ref(r_feature_emb, L0_rec_bilinear_W)
    return y

_drawn_inputs = setup_inputs


def setup_inputs(seed=0):
    import zlib

    import numpy as np

    out = dict(_drawn_inputs(seed))
    spreads = {}
    factors = {}
    for name, (base, spread) in spreads.items():
        noise = np.random.default_rng([zlib.crc32(name.encode()), seed]).standard_normal(out[name].shape)
        drawn = base * np.exp(spread * noise) if base else spread * noise
        out[name] = jnp.asarray(drawn.astype(out[name].dtype))
    for name, factor in factors.items():
        out[name] = (out[name] * factor).astype(out[name].dtype)
    return out
```

```python
import numpy as np
import concourse.bass as bass
from concourse import mybir
from contextlib import ExitStack


def bilinear_interaction_kernel(
    nc: bass.Bass,
    x: bass.AP,
    w_common: bass.AP,
    w_next: bass.AP,
    out: bass.AP,
):
    fp32 = mybir.dt.float32
    ALU = mybir.AluOpType

    B, F, D = x.shape
    ROWS = 128
    TILES = B // ROWS
    DUOS = F // 2
    BANK = 512
    PER_BANK = BANK // D
    SLOT_BANKS = 2
    SLOTS = 4
    SLOT_PAIRS = SLOT_BANKS * PER_BANK
    TURNS = 2
    DUOS_PER_TURN = DUOS // TURNS
    STAGES = 5

    def pairs_of(field):
        return F - 1 - field

    def first_pair(field):
        return sum(pairs_of(f) for f in range(field))

    def w_start(k):
        return sum(pairs_of(2 * m) for m in range(k))

    def units_of(field):
        n = pairs_of(field)
        parts = max(1, -(-n // SLOT_PAIRS))
        cuts = [-(-n * p // parts) for p in range(parts + 1)]
        return [(field, cuts[p], cuts[p + 1] - cuts[p]) for p in range(parts)] if n else []

    def couples_of(k):
        even, odd = units_of(2 * k), units_of(2 * k + 1)
        return [[u[c] for u in (even, odd) if c < len(u)] for c in range(max(len(even), len(odd)))]

    TURN_AFTER = [DUOS // 2 - 1, DUOS // 2]
    steps = []
    entries = []
    for k in range(DUOS):
        for couple in couples_of(k):
            made = []
            for u in couple:
                made.append((u, len([e for e in entries if e is not None]), len(entries)))
                entries.append(made[-1][1])
            steps.append(("couple", k, made))
        if k in TURN_AFTER:
            steps.append(("turn", TURN_AFTER.index(k), len(entries)))
            entries.append(None)
    UNITS = len([e for e in entries if e is not None])
    assert len(entries) % SLOTS == 0
    units = [u for kind, _, made in steps if kind == "couple" for u in made]

    ready_count = {}
    for kind, _, made in steps:
        if kind == "couple":
            for _, number, _ in sorted(made, key=lambda m: -(-m[0][2] // PER_BANK)):
                ready_count[number] = len(ready_count) + 1

    CHUNKS = [[k] for k in range(8)] + [[8, 9], list(range(10, DUOS))]
    chunk_of = {k: c for c, ks in enumerate(CHUNKS) for k in ks}
    chunk_first = [first_pair(2 * ks[0]) for ks in CHUNKS]
    chunk_pairs = [sum(pairs_of(2 * k) + pairs_of(2 * k + 1) for k in ks) for ks in CHUNKS]
    chunk_last_unit = [max(n for (f, _, _), n, _ in units if chunk_of[f // 2] == c) for c in range(len(CHUNKS))]
    STAGE_PAIRS = max(chunk_pairs)
    ROUNDS = len(CHUNKS) // STAGES
    assert len(CHUNKS) % STAGES == 0

    x_v = x.rearrange("(t b) f d -> t b (f d)", b=ROWS)
    out_v = out.rearrange("(t b) p d -> t b (p d)", b=ROWS)

    with ExitStack() as ctx:
        def sb(name, shape):
            return ctx.enter_context(nc.sbuf_tensor(name, shape, fp32))

        def sem(name):
            return ctx.enter_context(nc.semaphore(name))

        w_sb = sb("w_sb", [2 * D, w_start(DUOS) * D])
        x_sb = [sb(f"x_sb{s}", [ROWS, F * D]) for s in range(2)]
        xT = [sb(f"xT{s}", [2 * D, DUOS * ROWS]) for s in range(2)]
        stage = [sb(f"stage{s}", [ROWS, STAGE_PAIRS * D]) for s in range(STAGES)]
        ident = sb("ident", [ROWS, ROWS])
        slot = [ctx.enter_context(nc.psum_tensor(f"slot{s}", [ROWS, SLOT_BANKS * BANK], fp32))
                for s in range(SLOTS)]

        ident_zero = sem("ident_zero")
        ident_ready = sem("ident_ready")
        w_loaded = [sem(f"w_loaded{k}") for k in range(DUOS)]
        x_loaded = [sem(f"x_loaded{s}") for s in range(2)]
        turned = sem("turned")
        xT_ready = sem("xT_ready")
        products_ready = sem("products_ready")
        units_done = sem("units_done")
        stored = [sem(f"stored{s}") for s in range(STAGES)]

        block = ctx.enter_context(nc.Block())

        def over_tiles(eng, tile):
            tile(0, 1, 0)
            with eng.Fori(0, TILES // 2 - 1) as i:
                tile(2 * i + 1, i + 1, 1)
                tile(2 * i + 2, i + 2, 0)
            tile(TILES - 1, TILES // 2, 1)

        def is_first(t):
            return isinstance(t, int) and t == 0

        def is_last(t):
            return isinstance(t, int) and t == TILES - 1

        @block.gpsimd
        def _(pool):
            nc.gpsimd.memset(ident[:, :], 0.0).then_inc(ident_zero, 1)
            pool.wait_ge(ident_zero, 1)
            nc.gpsimd.affine_select(out=ident[:, :], in_=ident[:, :], compare_op=ALU.not_equal, fill=1.0,
                                    base=0, pattern=[[-1, ROWS]], channel_multiplier=1).then_inc(ident_ready, 1)

        @block.sync
        def _(sp):
            for k in range(DUOS):
                a, n = w_start(k), pairs_of(2 * k)
                if n > 1:
                    c = sum(pairs_of(2 * m + 1) for m in range(k))
                    sp.dma_start(w_sb[:, (a + 1) * D:(a + n) * D],
                                 w_common[:, c:c + n - 1, :].rearrange("r n d -> r (n d)")).then_inc(w_loaded[k], 16)
                sp.dma_start(w_sb[0:D, a * D:(a + 1) * D], w_next[:, k, :]).then_inc(w_loaded[k], 16)

            def tile(t, loads, s):
                for c in range(len(CHUNKS)):
                    sp.wait_ge(units_done, UNITS * t + chunk_last_unit[c] + 1)
                    a, n = chunk_first[c] * D, chunk_pairs[c] * D
                    sp.dma_start(out_v[t, :, a:a + n], stage[c % STAGES][:, 0:n]).then_inc(stored[c % STAGES], 16)

            over_tiles(sp, tile)
            for s in range(STAGES):
                sp.wait_ge(stored[s], 16 * ROUNDS * TILES)

        @block.scalar
        def _(act):
            def load_x(t, s):
                act.dma_start(x_sb[s][:, :], x_v[t, :, :]).then_inc(x_loaded[s], 16)

            def copy_turn(count, part, place, s):
                act.wait_ge(turned, count)
                n = DUOS_PER_TURN * ROWS
                nc.scalar.copy(xT[s][:, part * n:(part + 1) * n], slot[place % SLOTS][:, 0:n]).then_inc(xT_ready, 1)

            load_x(0, 0)
            for part in range(TURNS):
                copy_turn(part + 1, part, part - TURNS, 0)

            def tile(t, loads, s):
                if is_last(t):
                    return
                if not is_first(t):
                    act.wait_ge(units_done, UNITS * t)
                load_x(t + 1, 1 - s)
                for kind, part, place in steps:
                    if kind == "turn":
                        copy_turn(TURNS * (t + 1) + part + 1, part, place, 1 - s)

            over_tiles(act, tile)

        @block.tensor
        def _(pe):
            def turn(part, place, s):
                for m in range(DUOS_PER_TURN):
                    k = part * DUOS_PER_TURN + m
                    last = nc.tensor.transpose(slot[place % SLOTS][:, m * ROWS:(m + 1) * ROWS],
                                               x_sb[s][:, 2 * D * k:2 * D * (k + 1)], ident[:, :])
                last.then_inc(turned, 1)

            pe.wait_ge(ident_ready, 1)
            pe.wait_ge(x_loaded[0], 16)
            for part in range(TURNS):
                turn(part, part - TURNS, 0)

            def slot_is_free(t, e):
                before = e - SLOTS
                if before < 0:
                    if is_first(t):
                        return
                    n = UNITS * t + before + 1
                elif entries[before] is not None:
                    n = UNITS * t + entries[before] + 1
                else:
                    if not is_last(t):
                        pe.wait_ge(xT_ready, TURNS * (t + 1) + TURN_STEPS[before] + 1)
                        return
                    n = UNITS * t + entries[before - SLOTS] + 1
                pe.wait_ge(units_done, n)

            TURN_STEPS = {place: part for kind, part, place in steps if kind == "turn"}

            def couple(t, s, k, made):
                for _, _, place in made:
                    slot_is_free(t, place)
                for b in range(SLOT_BANKS):
                    for (field, first, n), number, place in made:
                        lo, hi = b * PER_BANK, min(n, (b + 1) * PER_BANK)
                        if lo >= hi:
                            continue
                        r = D * (field % 2)
                        a = w_start(k) + field % 2 + first
                        done = nc.tensor.matmul(slot[place % SLOTS][:, lo * D:hi * D],
                                                xT[s][r:r + D, k * ROWS:(k + 1) * ROWS],
                                                w_sb[r:r + D, (a + lo) * D:(a + hi) * D], start=True, stop=True)
                        if hi == n:
                            done.then_inc(products_ready, 1)

            def tile(t, loads, s):
                pe.wait_ge(xT_ready, TURNS * (t + 1))
                seen = set()
                for kind, what, rest in steps:
                    if kind == "couple":
                        if what not in seen:
                            seen.add(what)
                            pe.wait_ge(w_loaded[what], 16 * (2 if pairs_of(2 * what) > 1 else 1))
                        couple(t, s, what, rest)
                    elif not is_last(t):
                        if what == 0:
                            pe.wait_ge(x_loaded[1 - s], 16 * (loads + s))
                        slot_is_free(t, rest)
                        turn(what, rest, 1 - s)

            over_tiles(pe, tile)

        @block.vector
        def _(dve):
            def tile(t, loads, s):
                seen = set()
                dve.wait_ge(x_loaded[s], 16 * loads)
                for (field, first, n), number, place in units:
                    c = chunk_of[field // 2]
                    if c not in seen:
                        seen.add(c)
                        if not is_first(t) or c >= STAGES:
                            dve.wait_ge(stored[c % STAGES], 16 * (ROUNDS * t + c // STAGES))
                    dve.wait_ge(products_ready, UNITS * t + ready_count[number])
                    a = first_pair(field) + first - chunk_first[c]
                    j = field + 1 + first
                    nc.vector.tensor_tensor(stage[c % STAGES][:, a * D:(a + n) * D],
                                            slot[place % SLOTS][:, 0:n * D],
                                            x_sb[s][:, j * D:(j + n) * D], ALU.mult).then_inc(units_done, 1)

            over_tiles(dve, tile)


def kernel(r_feature_emb, L0_rec_bilinear_W):
    import concourse.bacc as _bacc
    from concourse import mybir as _mybir
    from concourse.bass_utils import run_bass_kernel_spmd as _run

    x = np.ascontiguousarray(r_feature_emb)
    w = np.asarray(L0_rec_bilinear_W)
    F = x.shape[1]
    number = {}
    for i in range(F):
        for j in range(i + 1, F):
            number[i, j] = len(number)
    even = [number[2 * k, j] for k in range(F // 2) for j in range(2 * k + 2, F)]
    odd = [number[2 * k + 1, j] for k in range(F // 2) for j in range(2 * k + 2, F)]
    nxt = [number[2 * k, 2 * k + 1] for k in range(F // 2)]
    w_common = np.ascontiguousarray(np.concatenate([w[even].transpose(1, 0, 2), w[odd].transpose(1, 0, 2)], axis=0))
    w_next = np.ascontiguousarray(w[nxt].transpose(1, 0, 2))

    nc = _bacc.Bacc("TRN2", target_bir_lowering=False, num_devices=1)
    arrays, args = {}, []
    for name, a in (("x", x), ("w_common", w_common), ("w_next", w_next)):
        arrays[name] = a
        args.append(nc.dram_tensor(name, a.shape, _mybir.dt.from_np(a.dtype), kind="ExternalInput").ap())
    out = nc.dram_tensor("out", (x.shape[0], len(number), x.shape[2]), _mybir.dt.from_np(x.dtype),
                         kind="ExternalOutput").ap()
    bilinear_interaction_kernel(nc, *args, out)
    r = _run(nc, [arrays], core_ids=[0])
    return r.results[0]["out"]
```

```python
import numpy as np
import concourse.bass as bass
from concourse import mybir
from contextlib import ExitStack


def bilinear_interaction_kernel(
    nc: bass.Bass,
    x: bass.AP,
    w_common: bass.AP,
    w_next: bass.AP,
    out: bass.AP,
):
    fp32 = mybir.dt.float32
    fp32r = mybir.dt.float32r
    ALU = mybir.AluOpType

    B, F, D = x.shape
    PAIRS = F * (F - 1) // 2
    ROWS = 128
    TILES = B // ROWS
    DUOS = F // 2
    BANK = 512
    PER_BANK = BANK // D
    SLOT_BANKS = 2
    SLOTS = 3
    TURN_BANKS = 2
    XT_DUOS = 4
    AHEAD = 2
    SPLITS = 2
    RAWS = 2
    STAGES = 5
    CHUNK_PAIRS = F - 1

    def pairs_of(field):
        return F - 1 - field

    def first_pair(field):
        return sum(pairs_of(f) for f in range(field))

    def fields_of(k):
        return [f for f in (2 * k, 2 * k + 1) if pairs_of(f)]

    SINGLE = 14
    units = []
    for field in range(F - 1):
        n = pairs_of(field)
        cut = n if n <= SINGLE else (n + 1) // 2
        units.append((field, 0, cut))
        if cut < n:
            units.append((field, cut, n - cut))
    UNITS = len(units)
    assert UNITS % SLOTS == 0 and max(n for _, _, n in units) <= SLOT_BANKS * PER_BANK

    chunks = []
    for field in range(F - 1):
        if chunks and sum(pairs_of(f) for f in chunks[-1]) + pairs_of(field) <= CHUNK_PAIRS:
            chunks[-1].append(field)
        else:
            chunks.append([field])
    CHUNKS = len(chunks)
    chunk_of = {f: c for c, fields in enumerate(chunks) for f in fields}
    chunk_units = [sum(chunk_of[f] <= c for f, _, _ in units) for c in range(CHUNKS)]
    ROUNDS = CHUNKS // STAGES
    assert CHUNKS % STAGES == 0 and DUOS % XT_DUOS == 0 and DUOS % SPLITS == 0

    x_v = x.rearrange("(t b) f d -> t b (f d)", b=ROWS)
    out_v = out.rearrange("(t b) p d -> t b (p d)", b=ROWS)

    with ExitStack() as ctx:
        def sb(name, shape, dt=fp32):
            return ctx.enter_context(nc.sbuf_tensor(name, shape, dt))

        def sem(name):
            return ctx.enter_context(nc.semaphore(name))

        w_sb = sb("w_sb", [2 * D, PAIRS * D], fp32r)
        w_raw = [sb(f"w_raw{r}", [2 * D, (F - 1) * D]) for r in range(RAWS)]
        x_sb = [sb(f"x_sb{s}", [ROWS, F * D]) for s in range(2)]
        x_hi = [sb(f"x_hi{g}", [ROWS, 2, 2, D], fp32r) for g in range(SPLITS)]
        x_lo = [sb(f"x_lo{g}", [ROWS, 2, 2, D]) for g in range(SPLITS)]
        xT = [sb(f"xT{q}", [2 * D, 2 * 2 * ROWS], fp32r) for q in range(XT_DUOS)]
        stage = [sb(f"stage{s}", [ROWS, CHUNK_PAIRS * D]) for s in range(STAGES)]
        ident = sb("ident", [ROWS, ROWS])
        slot = [ctx.enter_context(nc.psum_tensor(f"slot{s}", [ROWS, SLOT_BANKS * BANK], fp32))
                for s in range(SLOTS)]
        turn_bank = [ctx.enter_context(nc.psum_tensor(f"turn_bank{s}", [ROWS, BANK], fp32))
                     for s in range(TURN_BANKS)]

        ident_zero = sem("ident_zero")
        ident_ready = sem("ident_ready")
        raw_loaded = [sem(f"raw_loaded{r}") for r in range(RAWS)]
        w_hi_ready = sem("w_hi_ready")
        w_ready = sem("w_ready")
        x_loaded = [sem(f"x_loaded{s}") for s in range(2)]
        x_hi_ready = sem("x_hi_ready")
        x_lo_ready = sem("x_lo_ready")
        turned = sem("turned")
        xT_ready = sem("xT_ready")
        products_ready = sem("products_ready")
        units_done = sem("units_done")
        stored = [sem(f"stored{s}") for s in range(STAGES)]

        block = ctx.enter_context(nc.Block())

        def over_tiles(eng, tile):
            tile(0, 1, 0)
            with eng.Fori(0, TILES // 2 - 1) as i:
                tile(2 * i + 1, i + 1, 1)
                tile(2 * i + 2, i + 2, 0)
            tile(TILES - 1, TILES // 2, 1)

        def duo_twice(s, k):
            fields = x_sb[s][:, 2 * k * D:2 * (k + 1) * D].rearrange("b (f d) -> b f d", d=D)
            return fields.unsqueeze(2).to_broadcast([ROWS, 2, 2, D])

        def wrapped(t, loads, s, k):
            if k < DUOS:
                return t, loads, s, k
            return None if is_last(t) else (t + 1, loads + s, 1 - s, k - DUOS)

        def is_first(t):
            return isinstance(t, int) and t == 0

        def is_last(t):
            return isinstance(t, int) and t == TILES - 1

        def loads_of_raw(k):
            return sum(16 * len(fields_of(m)) for m in range(k % RAWS, k + 1, RAWS))

        @block.sync
        def _(sp):
            def load_x(t, s):
                sp.dma_start(x_sb[s][:, :], x_v[t, :, :]).then_inc(x_loaded[s], 16)

            def load_w(k):
                if k >= RAWS:
                    sp.wait_ge(w_ready, k - RAWS + 1)
                n = pairs_of(2 * k)
                raw = w_raw[k % RAWS]
                if n > 1:
                    c = sum(pairs_of(2 * m + 1) for m in range(k))
                    sp.dma_start(raw[:, D:n * D],
                                 w_common[:, c:c + n - 1, :].rearrange("r n d -> r (n d)")
                                 ).then_inc(raw_loaded[k % RAWS], 16)
                sp.dma_start(raw[0:D, 0:D], w_next[:, k, :]).then_inc(raw_loaded[k % RAWS], 16)

            load_x(0, 0)
            load_w(0)
            load_w(1)
            load_x(1, 1)
            load_w(2)
            load_w(3)

            def tile(t, loads, s):
                if not is_first(t) and not is_last(t):
                    sp.wait_ge(units_done, UNITS * t)
                    load_x(t + 1, 1 - s)
                w_next_duo = 2 * RAWS
                for c, fields in enumerate(chunks):
                    sp.wait_ge(units_done, UNITS * t + chunk_units[c])
                    a, n = first_pair(fields[0]) * D, sum(pairs_of(f) for f in fields) * D
                    sp.dma_start(out_v[t, :, a:a + n], stage[c % STAGES][:, 0:n]).then_inc(stored[c % STAGES], 16)
                    while is_first(t) and w_next_duo < DUOS and 2 * (w_next_duo - 2 * RAWS) + 1 <= fields[-1]:
                        load_w(w_next_duo)
                        w_next_duo += 1

            over_tiles(sp, tile)
            for s in range(STAGES):
                sp.wait_ge(stored[s], 16 * ROUNDS * TILES)

        @block.gpsimd
        def _(pool):
            nc.gpsimd.memset(ident[:, :], 0.0).then_inc(ident_zero, 1)
            pool.wait_ge(ident_zero, 1)
            nc.gpsimd.affine_select(out=ident[:, :], in_=ident[:, :], compare_op=ALU.not_equal, fill=1.0,
                                    base=0, pattern=[[-1, ROWS]], channel_multiplier=1).then_inc(ident_ready, 1)

            def tile(t, loads, s):
                for k in range(DUOS):
                    pool.wait_ge(x_hi_ready, DUOS * t + k + 1)
                    nc.gpsimd.tensor_tensor(x_lo[k % SPLITS][:, :, :, :], duo_twice(s, k),
                                            x_hi[k % SPLITS][:, :, :, :].bitcast(fp32),
                                            ALU.subtract).then_inc(x_lo_ready, 1)

            over_tiles(pool, tile)

        @block.scalar
        def _(act):
            def split_x(t, loads, s, k):
                if k == 0:
                    act.wait_ge(x_loaded[s], 16 * loads)
                if not is_first(t) or k >= SPLITS:
                    act.wait_ge(turned, DUOS * t + k - SPLITS + 1)
                nc.scalar.copy(x_hi[k % SPLITS][:, :, :, :], duo_twice(s, k)).then_inc(x_hi_ready, 1)

            def copy_turn(t, k):
                act.wait_ge(turned, DUOS * t + k + 1)
                n = 2 * ROWS * len(fields_of(k))
                nc.scalar.copy(xT[k % XT_DUOS][:, 0:n], turn_bank[k % TURN_BANKS][:, 0:n]).then_inc(xT_ready, 1)

            def split_w(k):
                act.wait_ge(raw_loaded[k % RAWS], loads_of_raw(k))
                for field in fields_of(k):
                    r = D * (field % 2)
                    a, n = first_pair(field) * D, pairs_of(field) * D
                    done = nc.scalar.copy(w_sb[r:r + D, a:a + n], w_raw[k % RAWS][r:r + D, r:r + n])
                done.then_inc(w_hi_ready, 1)

            def step(t, loads, s, k):
                if at := wrapped(t, loads, s, k):
                    copy_turn(at[0], at[3])
                if at := wrapped(t, loads, s, k + SPLITS):
                    split_x(*at)

            for k in range(SPLITS):
                split_x(0, 1, 0, k)
            for k in range(AHEAD):
                split_w(k)
                step(0, 1, 0, k)

            def tile(t, loads, s):
                for k in range(DUOS):
                    if is_first(t) and k + AHEAD < DUOS:
                        split_w(k + AHEAD)
                    step(t, loads, s, k + AHEAD)

            over_tiles(act, tile)

        @block.tensor
        def _(pe):
            pe.wait_ge(ident_ready, 1)

            def turn(t, k):
                pe.wait_ge(x_lo_ready, DUOS * t + k + 1)
                if not is_first(t) or k >= TURN_BANKS:
                    pe.wait_ge(xT_ready, DUOS * t + k - TURN_BANKS + 1)
                for m in range(len(fields_of(k))):
                    x_parts = x_lo[k % SPLITS][:, m, :, :], x_hi[k % SPLITS][:, m, :, :].bitcast(fp32)
                    for h, part in enumerate(x_parts):
                        c = (2 * m + h) * ROWS
                        done = nc.tensor.transpose(turn_bank[k % TURN_BANKS][:, c:c + ROWS],
                                                   part.rearrange("b r d -> b (r d)"), ident[:, :])
                done.then_inc(turned, 1)

            def products(t, number, field, first, n):
                if not is_first(t) or number >= SLOTS:
                    pe.wait_ge(units_done, UNITS * t + number - SLOTS + 1)
                k = field // 2
                for h in range(2):
                    c = (2 * (field % 2) + h) * ROWS
                    for lo in range(0, n, PER_BANK):
                        hi = min(n, lo + PER_BANK)
                        a = first_pair(field) + first
                        done = nc.tensor.matmul(slot[number % SLOTS][:, lo * D:hi * D],
                                                xT[k % XT_DUOS][:, c:c + ROWS],
                                                w_sb[:, (a + lo) * D:(a + hi) * D],
                                                start=(h == 0), stop=(h == 1))
                done.then_inc(products_ready, 1)

            for k in range(AHEAD):
                turn(0, k)

            def tile(t, loads, s):
                for k in range(DUOS):
                    if at := wrapped(t, loads, s, k + AHEAD):
                        turn(at[0], at[3])
                    pe.wait_ge(xT_ready, DUOS * t + k + 1)
                    if is_first(t):
                        pe.wait_ge(w_ready, k + 1)
                    for number, (field, first, n) in enumerate(units):
                        if field // 2 == k:
                            products(t, number, field, first, n)

            over_tiles(pe, tile)

        @block.vector
        def _(dve):
            def split_w(k):
                dve.wait_ge(w_hi_ready, k + 1)
                for field in fields_of(k):
                    r = D * (field % 2)
                    a, n = first_pair(field) * D, pairs_of(field) * D
                    done = nc.vector.tensor_tensor(w_sb[D - r:2 * D - r, a:a + n], w_raw[k % RAWS][r:r + D, r:r + n],
                                                   w_sb[r:r + D, a:a + n].bitcast(fp32), ALU.subtract)
                done.then_inc(w_ready, 1)

            for k in range(AHEAD):
                split_w(k)

            def tile(t, loads, s):
                dve.wait_ge(x_loaded[s], 16 * loads)
                for number, (field, first, n) in enumerate(units):
                    c = chunk_of[field]
                    if field == chunks[c][0] and first == 0 and (not is_first(t) or c >= STAGES):
                        dve.wait_ge(stored[c % STAGES], 16 * (ROUNDS * t + c // STAGES))
                    dve.wait_ge(products_ready, UNITS * t + number + 1)
                    a = first_pair(field) + first - first_pair(chunks[c][0])
                    j = field + 1 + first
                    nc.vector.tensor_tensor(stage[c % STAGES][:, a * D:(a + n) * D],
                                            slot[number % SLOTS][:, 0:n * D],
                                            x_sb[s][:, j * D:(j + n) * D], ALU.mult).then_inc(units_done, 1)
                    if is_first(t) and field % 2 and first + n == pairs_of(field) and field // 2 + AHEAD < DUOS:
                        split_w(field // 2 + AHEAD)

            over_tiles(dve, tile)


def kernel(r_feature_emb, L0_rec_bilinear_W):
    import concourse.bacc as _bacc
    from concourse import mybir as _mybir
    from concourse.bass_utils import run_bass_kernel_spmd as _run

    x = np.ascontiguousarray(r_feature_emb)
    w = np.asarray(L0_rec_bilinear_W)
    F = x.shape[1]
    number = {}
    for i in range(F):
        for j in range(i + 1, F):
            number[i, j] = len(number)
    even = [number[2 * k, j] for k in range(F // 2) for j in range(2 * k + 2, F)]
    odd = [number[2 * k + 1, j] for k in range(F // 2) for j in range(2 * k + 2, F)]
    nxt = [number[2 * k, 2 * k + 1] for k in range(F // 2)]
    w_common = np.ascontiguousarray(np.concatenate([w[even].transpose(1, 0, 2), w[odd].transpose(1, 0, 2)], axis=0))
    w_next = np.ascontiguousarray(w[nxt].transpose(1, 0, 2))

    nc = _bacc.Bacc("TRN2", target_bir_lowering=False, num_devices=1)
    arrays, args = {}, []
    for name, a in (("x", x), ("w_common", w_common), ("w_next", w_next)):
        arrays[name] = a
        args.append(nc.dram_tensor(name, a.shape, _mybir.dt.from_np(a.dtype), kind="ExternalInput").ap())
    out = nc.dram_tensor("out", (x.shape[0], len(number), x.shape[2]), _mybir.dt.from_np(x.dtype),
                         kind="ExternalOutput").ap()
    bilinear_interaction_kernel(nc, *args, out)
    r = _run(nc, [arrays], core_ids=[0])
    return r.results[0]["out"]
```

```python
import numpy as np
import concourse.bass as bass
from concourse import mybir
from contextlib import ExitStack


def bilinear_interaction_kernel(
    nc: bass.Bass,
    x: bass.AP,
    w_common: bass.AP,
    w_next: bass.AP,
    out: bass.AP,
):
    fp32 = mybir.dt.float32
    fp32r = mybir.dt.float32r
    ALU = mybir.AluOpType

    B, F, D = x.shape
    PAIRS = F * (F - 1) // 2
    ROWS = 128
    TILES = B // ROWS
    DUOS = F // 2
    BANK = 512
    PER_BANK = BANK // D
    SLOT_BANKS = 2
    SLOTS = 3
    TURN_BANKS = 2
    XT_DUOS = 4
    AHEAD = 2
    SPLITS = 2
    RAWS = 2
    STAGES = 5
    CHUNK_PAIRS = F - 1

    def pairs_of(field):
        return F - 1 - field

    def first_pair(field):
        return sum(pairs_of(f) for f in range(field))

    def fields_of(k):
        return [f for f in (2 * k, 2 * k + 1) if pairs_of(f)]

    SINGLE = 14
    units = []
    for field in range(F - 1):
        n = pairs_of(field)
        cut = n if n <= SINGLE else (n + 1) // 2
        units.append((field, 0, cut))
        if cut < n:
            units.append((field, cut, n - cut))
    UNITS = len(units)
    assert UNITS % SLOTS == 0 and max(n for _, _, n in units) <= SLOT_BANKS * PER_BANK

    HELP_EVERY = 8
    helped = [number for number in range(UNITS) if number % HELP_EVERY == HELP_EVERY // 2]
    HELPED = len(helped)

    def own_before(number):
        return number - helped_before(number)

    def helped_before(number):
        return sum(h < number for h in helped)

    OWN = own_before(UNITS)

    batches = []
    for k in range(DUOS):
        if batches and sum(pairs_of(2 * m) for m in batches[-1]) + pairs_of(2 * k) <= F - 1:
            batches[-1].append(k)
        else:
            batches.append([k])
    BATCHES = len(batches)
    batch_of = {k: b for b, duos in enumerate(batches) for k in duos}
    batch_at = {duos[0]: b for b, duos in enumerate(batches)}

    chunks = []
    for field in range(F - 1):
        if chunks and sum(pairs_of(f) for f in chunks[-1]) + pairs_of(field) <= CHUNK_PAIRS:
            chunks[-1].append(field)
        else:
            chunks.append([field])
    CHUNKS = len(chunks)
    chunk_of = {f: c for c, fields in enumerate(chunks) for f in fields}
    chunk_units = [sum(chunk_of[f] <= c for f, _, _ in units) for c in range(CHUNKS)]
    ROUNDS = CHUNKS // STAGES
    assert CHUNKS % STAGES == 0 and DUOS % XT_DUOS == 0 and DUOS % SPLITS == 0

    x_v = x.rearrange("(t b) f d -> t b (f d)", b=ROWS)
    out_v = out.rearrange("(t b) p d -> t b (p d)", b=ROWS)

    with ExitStack() as ctx:
        def sb(name, shape, dt=fp32):
            return ctx.enter_context(nc.sbuf_tensor(name, shape, dt))

        def sem(name):
            return ctx.enter_context(nc.semaphore(name))

        w_sb = sb("w_sb", [2 * D, PAIRS * D], fp32r)
        w_raw = [sb(f"w_raw{r}", [2 * D, (F - 1) * D]) for r in range(RAWS)]
        x_sb = [sb(f"x_sb{s}", [ROWS, F * D]) for s in range(2)]
        x_hi = [sb(f"x_hi{g}", [ROWS, 2, 2, D], fp32r) for g in range(SPLITS)]
        x_lo = [sb(f"x_lo{g}", [ROWS, 2, 2, D]) for g in range(SPLITS)]
        xT = [sb(f"xT{q}", [2 * D, 2 * 2 * ROWS], fp32r) for q in range(XT_DUOS)]
        stage = [sb(f"stage{s}", [ROWS, CHUNK_PAIRS * D]) for s in range(STAGES)]
        ident = sb("ident", [ROWS, ROWS])
        slot = [ctx.enter_context(nc.psum_tensor(f"slot{s}", [ROWS, SLOT_BANKS * BANK], fp32))
                for s in range(SLOTS)]
        turn_bank = [ctx.enter_context(nc.psum_tensor(f"turn_bank{s}", [ROWS, BANK], fp32))
                     for s in range(TURN_BANKS)]

        ident_zero = sem("ident_zero")
        ident_ready = sem("ident_ready")
        raw_loaded = [sem(f"raw_loaded{r}") for r in range(RAWS)]
        w_hi_ready = sem("w_hi_ready")
        w_ready = sem("w_ready")
        x_loaded = [sem(f"x_loaded{s}") for s in range(2)]
        x_hi_ready = sem("x_hi_ready")
        x_lo_ready = sem("x_lo_ready")
        turned = sem("turned")
        xT_ready = sem("xT_ready")
        products_ready = sem("products_ready")
        own_done = sem("own_done")
        helped_copied = sem("helped_copied")
        helped_done = sem("helped_done")
        stored = [sem(f"stored{s}") for s in range(STAGES)]

        block = ctx.enter_context(nc.Block())

        def over_tiles(eng, tile):
            tile(0, 1, 0)
            with eng.Fori(0, TILES // 2 - 1) as i:
                tile(2 * i + 1, i + 1, 1)
                tile(2 * i + 2, i + 2, 0)
            tile(TILES - 1, TILES // 2, 1)

        def duo_twice(s, k):
            fields = x_sb[s][:, 2 * k * D:2 * (k + 1) * D].rearrange("b (f d) -> b f d", d=D)
            return fields.unsqueeze(2).to_broadcast([ROWS, 2, 2, D])

        def place_of(field, first, n):
            c = chunk_of[field]
            a = first_pair(field) + first - first_pair(chunks[c][0])
            return stage[c % STAGES][:, a * D:(a + n) * D]

        def wait_for_stage(eng, t, field):
            c = chunk_of[field]
            if not is_first(t) or c >= STAGES:
                eng.wait_ge(stored[c % STAGES], 16 * (ROUNDS * t + c // STAGES))

        def wrapped(t, loads, s, k):
            if k < DUOS:
                return t, loads, s, k
            return None if is_last(t) else (t + 1, loads + s, 1 - s, k - DUOS)

        def is_first(t):
            return isinstance(t, int) and t == 0

        def is_last(t):
            return isinstance(t, int) and t == TILES - 1

        def raw_at(k):
            return sum(pairs_of(2 * m) for m in batches[batch_of[k]] if m < k) * D

        def raw_loads(b):
            return 16 * sum(len(fields_of(k)) for m in range(b % RAWS, b + 1, RAWS) for k in batches[m])

        def w_halves(b):
            for k in batches[b]:
                for field in fields_of(k):
                    r, n = D * (field % 2), pairs_of(field) * D
                    a, c = first_pair(field) * D, raw_at(k) + r
                    yield (w_raw[b % RAWS][r:r + D, c:c + n], w_sb[r:r + D, a:a + n],
                           w_sb[D - r:2 * D - r, a:a + n])

        @block.sync
        def _(sp):
            def load_x(t, s):
                sp.dma_start(x_sb[s][:, :], x_v[t, :, :]).then_inc(x_loaded[s], 16)

            def load_w(b):
                if b >= RAWS:
                    sp.wait_ge(w_ready, b - RAWS + 1)
                for k in batches[b]:
                    a, n = raw_at(k), pairs_of(2 * k) * D
                    if n > D:
                        c = sum(pairs_of(2 * m + 1) for m in range(k))
                        sp.dma_start(w_raw[b % RAWS][:, a + D:a + n],
                                     w_common[:, c:c + n // D - 1, :].rearrange("r n d -> r (n d)")
                                     ).then_inc(raw_loaded[b % RAWS], 16)
                    sp.dma_start(w_raw[b % RAWS][0:D, a:a + D], w_next[:, k, :]).then_inc(raw_loaded[b % RAWS], 16)

            load_w(0)
            load_x(0, 0)
            load_w(1)
            load_x(1, 1)
            load_w(2)
            load_w(3)

            def tile(t, loads, s):
                if not is_first(t) and not is_last(t):
                    load_x(t + 1, 1 - s)
                batch = 2 * RAWS
                for c, fields in enumerate(chunks):
                    own = OWN * t + own_before(chunk_units[c])
                    if helped_before(chunk_units[c]) > (helped_before(chunk_units[c - 1]) if c else 0):
                        of_helped = HELPED * t + helped_before(chunk_units[c])
                        of_helped = of_helped if isinstance(t, int) else sp.to_reg(of_helped)
                        sp.wait_ge(own_done, own)
                        sp.wait_ge(helped_done, of_helped)
                    else:
                        sp.wait_ge(own_done, own)
                    a, n = first_pair(fields[0]) * D, sum(pairs_of(f) for f in fields) * D
                    sp.dma_start(out_v[t, :, a:a + n], stage[c % STAGES][:, 0:n]).then_inc(stored[c % STAGES], 16)
                    while (is_first(t) and batch < BATCHES
                           and 2 * (batches[batch - RAWS][0] - AHEAD) + 1 <= fields[-1]):
                        load_w(batch)
                        batch += 1

            over_tiles(sp, tile)
            for s in range(STAGES):
                sp.wait_ge(stored[s], 16 * ROUNDS * TILES)

        @block.gpsimd
        def _(pool):
            nc.gpsimd.memset(ident[:, :], 0.0).then_inc(ident_zero, 1)
            pool.wait_ge(ident_zero, 1)
            nc.gpsimd.affine_select(out=ident[:, :], in_=ident[:, :], compare_op=ALU.not_equal, fill=1.0,
                                    base=0, pattern=[[-1, ROWS]], channel_multiplier=1).then_inc(ident_ready, 1)

            def split_x(t, loads, s, k):
                pool.wait_ge(x_hi_ready, DUOS * t + k + 1)
                nc.gpsimd.tensor_tensor(x_lo[k % SPLITS][:, :, :, :], duo_twice(s, k),
                                        x_hi[k % SPLITS][:, :, :, :].bitcast(fp32),
                                        ALU.subtract).then_inc(x_lo_ready, 1)

            def help_with(t, s, number, field, first, n):
                pool.wait_ge(helped_copied, HELPED * t + helped_before(number) + 1)
                at, j = place_of(field, first, n), field + 1 + first
                nc.gpsimd.tensor_tensor(at, at, x_sb[s][:, j * D:(j + n) * D], ALU.mult).then_inc(helped_done, 1)

            for k in range(AHEAD + SPLITS):
                split_x(0, 1, 0, k)

            def tile(t, loads, s):
                for k in range(DUOS):
                    if at := wrapped(t, loads, s, k + AHEAD + SPLITS):
                        split_x(*at)
                    for number, (field, first, n) in enumerate(units):
                        if field // 2 == k and number in helped:
                            help_with(t, s, number, field, first, n)

            over_tiles(pool, tile)

        @block.scalar
        def _(act):
            def split_x(t, loads, s, k):
                if k == 0:
                    act.wait_ge(x_loaded[s], 16 * loads)
                if not is_first(t) or k >= SPLITS:
                    act.wait_ge(turned, DUOS * t + k - SPLITS + 1)
                nc.scalar.copy(x_hi[k % SPLITS][:, :, :, :], duo_twice(s, k)).then_inc(x_hi_ready, 1)

            def copy_turn(t, k):
                act.wait_ge(turned, DUOS * t + k + 1)
                n = 2 * ROWS * len(fields_of(k))
                nc.scalar.copy(xT[k % XT_DUOS][:, 0:n], turn_bank[k % TURN_BANKS][:, 0:n]).then_inc(xT_ready, 1)

            def split_w(b):
                act.wait_ge(raw_loaded[b % RAWS], raw_loads(b))
                for raw, high, low in w_halves(b):
                    done = nc.scalar.copy(high, raw)
                done.then_inc(w_hi_ready, 1)

            def help_with(t, number, field, first, n):
                wait_for_stage(act, t, field)
                act.wait_ge(products_ready, UNITS * t + number + 1)
                nc.scalar.copy(place_of(field, first, n), slot[number % SLOTS][:, 0:n * D]).then_inc(helped_copied, 1)

            def step(t, loads, s, k):
                if at := wrapped(t, loads, s, k):
                    copy_turn(at[0], at[3])
                if at := wrapped(t, loads, s, k + SPLITS):
                    split_x(*at)

            split_w(0)
            for k in range(SPLITS):
                split_x(0, 1, 0, k)
            step(0, 1, 0, 0)
            split_w(1)
            step(0, 1, 0, 1)

            def tile(t, loads, s):
                for k in range(DUOS):
                    if is_first(t) and k + AHEAD in batch_at:
                        split_w(batch_at[k + AHEAD])
                    step(t, loads, s, k + AHEAD)
                    for number, (field, first, n) in enumerate(units):
                        if field // 2 == k and number in helped:
                            help_with(t, number, field, first, n)

            over_tiles(act, tile)

        @block.tensor
        def _(pe):
            pe.wait_ge(ident_ready, 1)

            def turn(t, k):
                pe.wait_ge(x_lo_ready, DUOS * t + k + 1)
                if not is_first(t) or k >= TURN_BANKS:
                    pe.wait_ge(xT_ready, DUOS * t + k - TURN_BANKS + 1)
                for m in range(len(fields_of(k))):
                    x_parts = x_lo[k % SPLITS][:, m, :, :], x_hi[k % SPLITS][:, m, :, :].bitcast(fp32)
                    for h, part in enumerate(x_parts):
                        c = (2 * m + h) * ROWS
                        done = nc.tensor.transpose(turn_bank[k % TURN_BANKS][:, c:c + ROWS],
                                                   part.rearrange("b r d -> b (r d)"), ident[:, :])
                done.then_inc(turned, 1)

            def products(t, number, field, first, n):
                before = number - SLOTS
                if (before % UNITS) in helped:
                    if not is_first(t) or before >= 0:
                        pe.wait_ge(helped_copied, HELPED * t + helped_before(before) + 1 if before >= 0 else
                                   HELPED * (t - 1) + helped_before(before + UNITS) + 1)
                elif not is_first(t) or before >= 0:
                    pe.wait_ge(own_done, OWN * t + own_before(before) + 1 if before >= 0 else
                               OWN * (t - 1) + own_before(before + UNITS) + 1)
                k = field // 2
                for h in range(2):
                    c = (2 * (field % 2) + h) * ROWS
                    for lo in range(0, n, PER_BANK):
                        hi = min(n, lo + PER_BANK)
                        a = first_pair(field) + first
                        done = nc.tensor.matmul(slot[number % SLOTS][:, lo * D:hi * D],
                                                xT[k % XT_DUOS][:, c:c + ROWS],
                                                w_sb[:, (a + lo) * D:(a + hi) * D],
                                                start=(h == 0), stop=(h == 1))
                done.then_inc(products_ready, 1)

            for k in range(AHEAD):
                turn(0, k)

            def tile(t, loads, s):
                for k in range(DUOS):
                    if at := wrapped(t, loads, s, k + AHEAD):
                        turn(at[0], at[3])
                    pe.wait_ge(xT_ready, DUOS * t + k + 1)
                    if is_first(t) and k in batch_at:
                        pe.wait_ge(w_ready, batch_at[k] + 1)
                    for number, (field, first, n) in enumerate(units):
                        if field // 2 == k:
                            products(t, number, field, first, n)

            over_tiles(pe, tile)

        @block.vector
        def _(dve):
            def split_w(b):
                dve.wait_ge(w_hi_ready, b + 1)
                for raw, high, low in w_halves(b):
                    done = nc.vector.tensor_tensor(low, raw, high.bitcast(fp32), ALU.subtract)
                done.then_inc(w_ready, 1)

            for b in range(AHEAD):
                split_w(b)

            def tile(t, loads, s):
                dve.wait_ge(x_loaded[s], 16 * loads)
                for number, (field, first, n) in enumerate(units):
                    if number not in helped:
                        wait_for_stage(dve, t, field)
                        dve.wait_ge(products_ready, UNITS * t + number + 1)
                        j = field + 1 + first
                        nc.vector.tensor_tensor(place_of(field, first, n), slot[number % SLOTS][:, 0:n * D],
                                                x_sb[s][:, j * D:(j + n) * D], ALU.mult).then_inc(own_done, 1)
                    if is_first(t) and field % 2 and first + n == pairs_of(field) and field // 2 + AHEAD in batch_at:
                        split_w(batch_at[field // 2 + AHEAD])

            over_tiles(dve, tile)


def kernel(r_feature_emb, L0_rec_bilinear_W):
    import concourse.bacc as _bacc
    from concourse import mybir as _mybir
    from concourse.bass_utils import run_bass_kernel_spmd as _run

    x = np.ascontiguousarray(r_feature_emb)
    w = np.asarray(L0_rec_bilinear_W)
    F = x.shape[1]
    number = {}
    for i in range(F):
        for j in range(i + 1, F):
            number[i, j] = len(number)
    even = [number[2 * k, j] for k in range(F // 2) for j in range(2 * k + 2, F)]
    odd = [number[2 * k + 1, j] for k in range(F // 2) for j in range(2 * k + 2, F)]
    nxt = [number[2 * k, 2 * k + 1] for k in range(F // 2)]
    w_common = np.ascontiguousarray(np.concatenate([w[even].transpose(1, 0, 2), w[odd].transpose(1, 0, 2)], axis=0))
    w_next = np.ascontiguousarray(w[nxt].transpose(1, 0, 2))

    nc = _bacc.Bacc("TRN2", target_bir_lowering=False, num_devices=1)
    arrays, args = {}, []
    for name, a in (("x", x), ("w_common", w_common), ("w_next", w_next)):
        arrays[name] = a
        args.append(nc.dram_tensor(name, a.shape, _mybir.dt.from_np(a.dtype), kind="ExternalInput").ap())
    out = nc.dram_tensor("out", (x.shape[0], len(number), x.shape[2]), _mybir.dt.from_np(x.dtype),
                         kind="ExternalOutput").ap()
    bilinear_interaction_kernel(nc, *args, out)
    r = _run(nc, [arrays], core_ids=[0])
    return r.results[0]["out"]
```
